# Optimizing a Trainium2 kernel written in Bass

```python
import numpy as np
import jax
import jax.numpy as jnp

def _softmax(x, axis=-1):
    return jax.nn.softmax(x, axis=axis)

def _gelu(x):
    return jax.nn.gelu(x, approximate=True)

def _silu(x):
    return jax.nn.silu(x)

def _sigmoid(x):
    return jax.nn.sigmoid(x)

def _layernorm(x, axis=-1, eps=1e-05):
    m = jnp.mean(x, axis=axis, keepdims=True)
    v = jnp.var(x, axis=axis, keepdims=True)
    return (x - m) / jnp.sqrt(v + eps)

def _scatter_add(tgt, idx, src, axis=0):
    return tgt.at[idx].add(src)

def _segment_sum(src, seg, n):
    return jax.ops.segment_sum(src, seg, n)
kernel_name = 'mk_gps_d1_gnn_r8_d6a648'

def setup_inputs(seed: int=0):
    np.random.seed(seed)
    _w = jnp.asarray

    def _rec_inputs():
        import jax
        import jax.numpy as jnp
        _gk = jax.random.key(seed)
        x = -0.000202 + 1 * jax.random.normal(jax.random.fold_in(_gk, 1), (6250, 256), jnp.float32)
        _s = jax.random.randint(jax.random.fold_in(_gk, 2), (50000,), 0, 6250, jnp.int32)
        _d = jax.random.randint(jax.random.fold_in(_gk, 3), (50000,), 0, 6250, jnp.int32)
        _loop = jnp.arange(6250, dtype=jnp.int32)
        src = jnp.concatenate([_s, _d, _loop])
        dst = jnp.concatenate([_d, _s, _loop])
        _o = jnp.argsort(dst, stable=True)
        src = src[_o]
        dst = dst[_o]
        return (x, src, dst)
    x, src, dst = _rec_inputs()

    def _L0_gnn_setup():
        import jax, jax.numpy as jnp
        import numpy as np
        N_NODES = 3125
        N_EDGES = 50000
        D_IN = 256
        D_OUT = 256
        HEADS = 8
        HEAD_DIM = D_OUT // HEADS
        NEG_SLOPE = 0.2
        LN_EPS = 1e-05

        def layer_norm(x, g, b):
            mu = jnp.mean(x, axis=-1, keepdims=True)
            var = jnp.mean((x - mu) ** 2, axis=-1, keepdims=True)
            return (x - mu) * jax.lax.rsqrt(var + LN_EPS) * g + b

        def gelu_tanh(x):
            c = np.sqrt(2.0 / np.pi).astype(np.float32)
            return 0.5 * x * (1.0 + jnp.tanh(c * (x + 0.044715 * x ** 3)))
        key = jax.random.key(seed)
        ks = jax.random.split(key, 16)
        s_in = 1.0 / np.sqrt(D_IN)
        s_out = 1.0 / np.sqrt(D_OUT)
        s_ff = 1.0 / np.sqrt(4 * D_OUT)
        return {'x': jax.random.normal(ks[0], (N_NODES, D_IN), jnp.float32), 'edge_index': jax.random.randint(ks[1], (2, N_EDGES), 0, N_NODES, jnp.int64), 'W': jax.random.normal(ks[2], (D_IN, HEADS * HEAD_DIM), jnp.float32) * s_in, 'att_src': jax.random.normal(ks[3], (HEADS, HEAD_DIM), jnp.float32) * s_out, 'att_dst': jax.random.normal(ks[4], (HEADS, HEAD_DIM), jnp.float32) * s_out, 'bias': jnp.zeros((D_OUT,), jnp.float32), 'W_res': jax.random.normal(ks[5], (D_IN, D_OUT), jnp.float32) * s_in, 'ln1_g': jnp.ones((D_IN,), jnp.float32), 'ln1_b': jnp.zeros((D_IN,), jnp.float32), 'ln2_g': jnp.ones((D_OUT,), jnp.float32), 'ln2_b': jnp.zeros((D_OUT,), jnp.float32), 'ffn_w1': jax.random.normal(ks[6], (D_OUT, 4 * D_OUT), jnp.float32) * s_out, 'ffn_b1': jnp.zeros((4 * D_OUT,), jnp.float32), 'ffn_w2': jax.random.normal(ks[7], (4 * D_OUT, D_OUT), jnp.float32) * s_ff, 'ffn_b2': jnp.zeros((D_OUT,), jnp.float32)}
    _L0_gnn_all = _L0_gnn_setup()
    _L0_gnn_in = {k: v for k, v in _L0_gnn_all.items() if k in ('W', 'att_src', 'att_dst', 'bias', 'W_res', 'ln1_g', 'ln1_b', 'ln2_g', 'ln2_b', 'ffn_w1', 'ffn_b1', 'ffn_w2', 'ffn_b2')}
    del _L0_gnn_all

    def _L0_mix_setup():
        import math
        import jax, jax.numpy as jnp
        import numpy as np
        EPS_DIV = 1e-07
        EPS_NORM = 1e-12

        def _l2_normalize(x, axis):
            n = jnp.sqrt(jnp.sum(x * x, axis=axis, keepdims=True))
            return x / jnp.maximum(n, EPS_NORM)
        key = jax.random.key(seed)
        ks = jax.random.split(key, 5)
        b, N, C = (8, 512, 256)
        x = jax.random.normal(ks[0], (b, N, C), dtype=jnp.float32)
        W_qkv = jax.random.normal(ks[1], (C, 3 * C), dtype=jnp.float32) * (1.0 / math.sqrt(C))
        b_qkv = jax.random.normal(ks[2], (3 * C,), dtype=jnp.float32) * 0.02
        W_out = jax.random.normal(ks[3], (C, C), dtype=jnp.float32) * (1.0 / math.sqrt(C))
        b_out = jax.random.normal(ks[4], (C,), dtype=jnp.float32) * 0.02
        return {'x': x, 'W_qkv': W_qkv, 'b_qkv': b_qkv, 'W_out': W_out, 'b_out': b_out}
    _L0_mix_all = _L0_mix_setup()
    _L0_mix_in = {k: v for k, v in _L0_mix_all.items() if k in ('W_qkv', 'b_qkv', 'W_out', 'b_out')}
    del _L0_mix_all

    def _L0_ffn_setup():
        import jax, jax.numpy as jnp
        import numpy as np
        E = 8
        K = 2
        D = 256
        H = 512
        DOUT = 256
        EPS = 1e-05
        key = jax.random.key(seed)
        ks = jax.random.split(key, 9)
        s = 0.02
        return {'x': jax.random.normal(ks[0], (4, 1024, D), jnp.float32), 'gamma': 1.0 + 0.05 * jax.random.normal(ks[1], (D,), jnp.float32), 'beta': 0.05 * jax.random.normal(ks[2], (D,), jnp.float32), 'Wr': 0.01 * jax.random.normal(ks[3], (D, E), jnp.float32), 'br': jnp.zeros((E,), jnp.float32), 'W1': s * jax.random.normal(ks[4], (E, D, H), jnp.float32), 'b1': s * jax.random.normal(ks[5], (E, H), jnp.float32), 'W2': s * jax.random.normal(ks[6], (E, H, DOUT), jnp.float32), 'b2': s * jax.random.normal(ks[7], (E, DOUT), jnp.float32)}
    _L0_ffn_all = _L0_ffn_setup()
    _L0_ffn_in = {k: v for k, v in _L0_ffn_all.items() if k in ('gamma', 'beta', 'Wr', 'br', 'W1', 'b1', 'W2', 'b2')}
    del _L0_ffn_all
    return {'x': x, 'src': src, 'dst': dst, 'L0_gnn_W': _L0_gnn_in['W'], 'L0_gnn_att_src': _L0_gnn_in['att_src'], 'L0_gnn_att_dst': _L0_gnn_in['att_dst'], 'L0_gnn_bias': _L0_gnn_in['bias'], 'L0_gnn_W_res': _L0_gnn_in['W_res'], 'L0_gnn_ln1_g': _L0_gnn_in['ln1_g'], 'L0_gnn_ln1_b': _L0_gnn_in['ln1_b'], 'L0_gnn_ln2_g': _L0_gnn_in['ln2_g'], 'L0_gnn_ln2_b': _L0_gnn_in['ln2_b'], 'L0_gnn_ffn_w1': _L0_gnn_in['ffn_w1'], 'L0_gnn_ffn_b1': _L0_gnn_in['ffn_b1'], 'L0_gnn_ffn_w2': _L0_gnn_in['ffn_w2'], 'L0_gnn_ffn_b2': _L0_gnn_in['ffn_b2'], 'L0_mix_W_qkv': _L0_mix_in['W_qkv'], 'L0_mix_b_qkv': _L0_mix_in['b_qkv'], 'L0_mix_W_out': _L0_mix_in['W_out'], 'L0_mix_b_out': _L0_mix_in['b_out'], 'L0_ffn_gamma': _L0_ffn_in['gamma'], 'L0_ffn_beta': _L0_ffn_in['beta'], 'L0_ffn_Wr': _L0_ffn_in['Wr'], 'L0_ffn_br': _L0_ffn_in['br'], 'L0_ffn_W1': _L0_ffn_in['W1'], 'L0_ffn_b1': _L0_ffn_in['b1'], 'L0_ffn_W2': _L0_ffn_in['W2'], 'L0_ffn_b2': _L0_ffn_in['b2']}

def reference(x, src, dst, L0_gnn_W, L0_gnn_att_src, L0_gnn_att_dst, L0_gnn_bias, L0_gnn_W_res, L0_gnn_ln1_g, L0_gnn_ln1_b, L0_gnn_ln2_g, L0_gnn_ln2_b, L0_gnn_ffn_w1, L0_gnn_ffn_b1, L0_gnn_ffn_w2, L0_gnn_ffn_b2, L0_mix_W_qkv, L0_mix_b_qkv, L0_mix_W_out, L0_mix_b_out, L0_ffn_gamma, L0_ffn_beta, L0_ffn_Wr, L0_ffn_br, L0_ffn_W1, L0_ffn_b1, L0_ffn_W2, L0_ffn_b2):
    import jax
    import jax.numpy as jnp

    def _L0_gnn_ref(x, edge_index, W, att_src, att_dst, bias, W_res, ln1_g, ln1_b, ln2_g, ln2_b, ffn_w1, ffn_b1, ffn_w2, ffn_b2):
        import jax, jax.numpy as jnp
        import numpy as np
        N_NODES = 3125
        N_EDGES = 50000
        D_IN = 256
        D_OUT = 256
        HEADS = 8
        HEAD_DIM = D_OUT // HEADS
        NEG_SLOPE = 0.2
        LN_EPS = 1e-05

        def layer_norm(x, g, b):
            mu = jnp.mean(x, axis=-1, keepdims=True)
            var = jnp.mean((x - mu) ** 2, axis=-1, keepdims=True)
            return (x - mu) * jax.lax.rsqrt(var + LN_EPS) * g + b

        def gelu_tanh(x):
            c = np.sqrt(2.0 / np.pi).astype(np.float32)
            return 0.5 * x * (1.0 + jnp.tanh(c * (x + 0.044715 * x ** 3)))
        N = x.shape[0]
        xn = layer_norm(x, ln1_g, ln1_b)
        loops = jnp.arange(N, dtype=edge_index.dtype)
        src = jnp.concatenate([edge_index[0], loops])
        dst = jnp.concatenate([edge_index[1], loops])
        h = (xn @ W).reshape(N, HEADS, HEAD_DIM)
        a_src = jnp.einsum('nhd,hd->nh', h, att_src)
        a_dst = jnp.einsum('nhd,hd->nh', h, att_dst)
        e = jax.nn.leaky_relu(a_src[src] + a_dst[dst], NEG_SLOPE)
        emax = jax.ops.segment_max(e, dst, num_segments=N)
        ee = jnp.exp(e - emax[dst])
        denom = jax.ops.segment_sum(ee, dst, num_segments=N)
        alpha = ee / denom[dst]
        msg = h[src] * alpha[:, :, None]
        agg = jax.ops.segment_sum(msg, dst, num_segments=N)
        out = agg.reshape(N, HEADS * HEAD_DIM) + xn @ W_res + bias
        out = layer_norm(out, ln2_g, ln2_b)
        ff = gelu_tanh(out @ ffn_w1 + ffn_b1) @ ffn_w2 + ffn_b2
        return out + ff

    def _L0_mix_ref(x, W_qkv, b_qkv, W_out, b_out):
        import math
        import jax, jax.numpy as jnp
        import numpy as np
        EPS_DIV = 1e-07
        EPS_NORM = 1e-12

        def _l2_normalize(x, axis):
            n = jnp.sqrt(jnp.sum(x * x, axis=axis, keepdims=True))
            return x / jnp.maximum(n, EPS_NORM)
        b, N, C = x.shape
        qkv = x @ W_qkv + b_qkv
        q, k, v = jnp.split(qkv, 3, axis=2)
        q = q - jnp.mean(q, axis=2, keepdims=True)
        k = k - jnp.mean(k, axis=2, keepdims=True)
        q2 = q * q
        k2 = k * k
        q2s = jnp.sum(q2, axis=2, keepdims=True)
        k2s = jnp.sum(k2, axis=2, keepdims=True)
        k2 = _l2_normalize(k2 / (k2s + EPS_DIV), axis=-2)
        q2 = _l2_normalize(q2 / (q2s + EPS_DIV), axis=-1)
        kv = jnp.einsum('bnc,bnd->bcd', k2, v)
        t2 = jnp.einsum('bnc,bcd->bnd', q2, kv) / math.sqrt(N)
        attn = v + t2
        return attn @ W_out + b_out

    def _L0_ffn_ref(x, gamma, beta, Wr, br, W1, b1, W2, b2):
        import jax, jax.numpy as jnp
        import numpy as np
        E = 8
        K = 2
        D = 256
        H = 512
        DOUT = 256
        EPS = 1e-05
        mu = jnp.mean(x, axis=-1, keepdims=True)
        var = jnp.mean(jnp.square(x - mu), axis=-1, keepdims=True)
        xn = (x - mu) * jax.lax.rsqrt(var + EPS) * gamma + beta
        logits = jnp.einsum('bsd,de->bse', xn, Wr) + br
        top_vals, top_idx = jax.lax.top_k(logits, K)
        w = jax.nn.softmax(top_vals, axis=-1)
        w_full = jnp.einsum('bsk,bske->bse', w, jax.nn.one_hot(top_idx, E, dtype=w.dtype))
        y = jnp.zeros(x.shape[:-1] + (DOUT,), x.dtype)
        for e in range(E):
            h = jax.nn.gelu(jnp.einsum('bsd,dh->bsh', xn, W1[e]) + b1[e], approximate=False)
            y_e = jnp.einsum('bsh,hd->bsd', h, W2[e]) + b2[e]
            y = y + y_e * w_full[..., e, None]
        return y
    edge_index = jnp.stack([src, dst])
    xn = _layernorm(x, axis=-1)
    x = x + _L0_gnn_ref(xn, edge_index, L0_gnn_W, L0_gnn_att_src, L0_gnn_att_dst, L0_gnn_bias, L0_gnn_W_res, L0_gnn_ln1_g, L0_gnn_ln1_b, L0_gnn_ln2_g, L0_gnn_ln2_b, L0_gnn_ffn_w1, L0_gnn_ffn_b1, L0_gnn_ffn_w2, L0_gnn_ffn_b2) + _L0_mix_ref(xn[None], L0_mix_W_qkv, L0_mix_b_qkv, L0_mix_W_out, L0_mix_b_out)[0]
    x = x + _L0_ffn_ref(_layernorm(x, axis=-1)[None], L0_ffn_gamma, L0_ffn_beta, L0_ffn_Wr, L0_ffn_br, L0_ffn_W1, L0_ffn_b1, L0_ffn_W2, L0_ffn_b2)[0]
    return x

_drawn_inputs = setup_inputs


def setup_inputs(seed=0):
    import zlib

    import numpy as np

    out = dict(_drawn_inputs(seed))
    spreads = {'L0_gnn_bias': (0.0, 0.1),
     'L0_gnn_ln1_g': (1.0, 0.2),
     'L0_gnn_ln1_b': (0.0, 0.1),
     'L0_gnn_ln2_g': (1.0, 0.2),
     'L0_gnn_ln2_b': (0.0, 0.1),
     'L0_gnn_ffn_b1': (0.0, 0.1),
     'L0_gnn_ffn_b2': (0.0, 0.1),
     'L0_ffn_br': (0.0, 0.28)}
    factors = {'L0_gnn_att_dst': 3.477,
     'L0_mix_b_out': 5.334,
     'L0_ffn_gamma': 8.0,
     'L0_ffn_beta': 8.0,
     'L0_ffn_b1': 22.319,
     'L0_ffn_b2': 7.93}
    for name, (base, spread) in spreads.items():
        noise = np.random.default_rng([zlib.crc32(name.encode()), seed]).standard_normal(out[name].shape)
        drawn = base * np.exp(spread * noise) if base else spread * noise
        out[name] = jnp.asarray(drawn.astype(out[name].dtype))
    for name, factor in factors.items():
        out[name] = (out[name] * factor).astype(out[name].dtype)
    return out
```

```python
from contextlib import ExitStack

import numpy as np
import concourse.bass as bass
from concourse import mybir

F32 = mybir.dt.float32
BF16 = mybir.dt.bfloat16
I32 = mybir.dt.int32
U32 = mybir.dt.uint32
ALU = mybir.AluOpType
ACT = mybir.ActivationFunctionType
AX = mybir.AxisListType.X

P = 128
N = 6250
D = 256
E = 106250
H = 8
HD = D // H
NT = 125
T = N // NT
KD = D // P
PAIR = 2 * NT
GC = 4
CE = -(-E // P)
NG = -(-CE // GC)
RT = -(-CE // P)
CP = RT * P
CX = GC * (NG + 1)
FULL = E // P
B = 16
J = GC * NG // B
L = J * P
RING = 4
SENT = 8191
BIG = 3.0e38
SLOPE = 0.2
EPS = 1e-5
EPS_DIV = 1e-7
EPS_NORM = 1e-12
FF = 4 * D
FFC = FF // P
X = 8
XH = 512
XC = XH // P
AW = 2 * H
EW = 2 * H + 1
SW = D + EW
assert J * B == GC * NG and T * NT == N and T % 2 == 0


class Steps:

    def __init__(self, eng, sem, base=0):
        self.eng, self.sem, self.base, self.n = eng, sem, base, 0

    def after(self, ins):
        ins.then_inc(self.sem, 1)
        self.n += 1

    def wait(self):
        self.eng.wait_ge(self.sem, self.base + self.n)

    def do(self, ins):
        self.after(ins)
        self.wait()


def passed(eng, sem):
    eng.sem_inc(sem, 1)


def chunks_of(v, first):
    n = v.shape[0] - first
    tiles = n // (P * P)
    rest = n - tiles * P * P
    rows = rest // P
    parts = [(slice(0, P), slice(0, tiles), slice(0, P),
              v[first:first + tiles * P * P].rearrange("(k q p) -> q k p", q=P, p=P))]
    at = first + tiles * P * P
    parts.append((slice(0, rows), tiles, slice(0, P), v[at:at + rows * P].rearrange("(q p) -> q p", p=P)))
    at += rows * P
    parts.append((slice(rows, rows + 1), tiles, slice(0, rest - rows * P), v[at:].rearrange("(a p) -> a p", a=1)))
    return parts


def row(v):
    return v.rearrange("(a n) -> a n", a=1)


def spread(v, p=P):
    return row(v).to_broadcast([p, v.shape[0]])


def columns(v, k):
    return v.rearrange("(k p) -> p k", k=k)


def gps_layer(nc, a):
    with ExitStack() as whole:
        def sem(name):
            return whole.enter_context(nc.semaphore(name))

        def allocate(stack, name, shape, dt=F32):
            return stack.enter_context(nc.sbuf_tensor(name, shape, dt))

        def scratch(name, shape):
            return nc.dram_tensor(name, shape, F32, kind="Internal").ap()

        c = dict(
            ident=allocate(whole, "ident", [P, P]),
            ones=allocate(whole, "ones", [P, P]),
            iota=allocate(whole, "iota", [P, NT]),
            tile_base=allocate(whole, "tile_base", [P, T]),
            lane8=allocate(whole, "lane8", [P, X]),
            meta=allocate(whole, "meta", [1, 2 * T + 1 + NG], I32),
            src=allocate(whole, "src_of", [P, CP], I32),
            dst=allocate(whole, "dst_of", [P, CP]),
            node_a=allocate(whole, "node_a", [NT, T, AW]),
            kvo=allocate(whole, "kvo", [P, KD, D]),
            edge=allocate(whole, "edge", [P, CX, EW]),
        )
        dram = dict(h=scratch("h_rows", [N, D]), asrc=scratch("a_src_rows", [N, H]), res=scratch("res_rows", [N, D]),
                    vox=scratch("vox_rows", [N, D]), q2t=scratch("q2_columns", [D, N]))
        with ExitStack() as softmax:
            c["last"] = allocate(softmax, "last_of", [P, CP])
            c["a_edge"] = allocate(softmax, "a_edge", [P, CX, H])
            prep(nc, a, c, sem)
            with ExitStack() as front:
                c["x0"] = allocate(front, "x0", [NT, T, D])
                gnn(nc, a, c, dram, sem)
                mix(nc, a, c, dram, sem)
            soft(nc, a, c, dram, sem)
        main(nc, a, c, dram, sem)


def short(name):
    return name.replace('L0_gnn_', '').replace('L0_mix_', '').replace('L0_ffn_', 'moe_')


def prep(nc, a, c, sem):
    with ExitStack() as ctx:
        def sb(name, shape, dt=F32):
            return ctx.enter_context(nc.sbuf_tensor(name, shape, dt))

        rows = [sb(f"rows{n}", [P, RT, P], I32) for n in range(3)]
        rowsf = [sb(f"rowsf{n}", [P, RT, P]) for n in range(3)]
        nxt = sb("nxt", [P, CP])
        ends = sb("ends", [1, 2, NG], I32)
        endsf = sb("endsf", [1, 2, NG])
        ii = sb("ii", [P, P], I32)
        thr = sb("thr", [P, 1])
        thr_hi = sb("thr_hi", [P, 1])
        below = sb("below", [T, 2, NG])
        cnt = sb("cnt", [T, 2])
        cnti = sb("cnti", [T, 2], I32)
        tri = sb("tri", [T, T + 1])
        rowm = sb("rowm", [1, 3 * T + 1])
        gi = sb("gi", [NG // 2, 2], I32)
        gf = sb("gf", [NG // 2, 2])
        mb = sb("mb", [NG // 2, 3 * T + 1])
        seen = sb("seen", [NG // 2, 2, T])
        seeni = sb("seeni", [NG // 2, 2, T], I32)
        mask = sb("mask", [NG // 2, 2, T])
        lastc = sb("lastc", [NG // 2, 2])
        ps_t = [ctx.enter_context(nc.psum_tensor(f"prep_turned_{n}", [P, 4, P], F32)) for n in range(2)]
        ps_m = ctx.enter_context(nc.psum_tensor("prep_sums", [P, 512], F32))
        s_fill, s_rows, s_ends = sem("prep_filled"), sem("prep_rows_in"), sem("prep_ends_in")
        s_pool, s_v, s_pe, s_tr, s_ev = (sem("prep_pool"), sem("prep_vector"), sem("prep_tensor"),
                                         sem("prep_turned"), sem("prep_evacuated"))
        block = ctx.enter_context(nc.Block())
        jobs = [(n, k) for n in range(3) for k in range(RT)]
        NDMA = 9

        @block.sync
        def _(sp):
            sp.wait_ge(s_fill, 4)
            with nc.allow_non_contiguous_dma(reason="first and last targets of the groups"):
                sp.dma_start(ends[0:1, 0, 0:NG], strided(a["dst"], 0, NG)).then_inc(s_ends, 16)
                sp.dma_start(ends[0:1, 1, 0:NG - 1], strided(a["dst"], GC * P - 1, NG - 1)).then_inc(s_ends, 16)
            for n, (v, first) in enumerate(((a["src"], 0), (a["dst"], 0), (a["dst"], 1))):
                for q, k, p, part in chunks_of(v, first):
                    sp.dma_start(rows[n][q, k, p], part).then_inc(s_rows, 16)
            sp.wait_ge(s_rows, 16 * NDMA)
            sp.wait_ge(s_ends, 32)

        @block.gpsimd
        def _(pool):
            st = Steps(pool, s_pool)
            st.after(pool.memset(c["ident"][:], 0.0))
            st.after(pool.memset(c["ones"][:], 1.0))
            st.after(pool.memset(tri[:], 0.0))
            st.wait()
            st.after(pool.affine_select(out=c["ident"][:], in_=c["ident"][:], compare_op=ALU.not_equal, fill=1.0,
                                        base=0, pattern=[[-1, P]], channel_multiplier=1))
            st.do(pool.affine_select(out=tri[:], in_=tri[:], compare_op=ALU.is_ge, fill=1.0,
                                     base=0, pattern=[[-1, T + 1]], channel_multiplier=1))
            st.do(pool.iota(ii[:, 0:NT], pattern=[[1, NT]], base=0, channel_multiplier=0))
            st.do(pool.tensor_copy(c["iota"][:], ii[:, 0:NT]))
            st.do(pool.iota(ii[:, 0:T], pattern=[[NT, T]], base=0, channel_multiplier=0))
            st.do(pool.tensor_copy(c["tile_base"][:], ii[:, 0:T]))
            st.do(pool.iota(ii[:, 0:X], pattern=[[1, X]], base=0, channel_multiplier=0))
            st.do(pool.tensor_copy(c["lane8"][:], ii[:, 0:X]))
            st.do(pool.iota(ii[:, 0:1], pattern=[[1, 1]], base=0, channel_multiplier=NT))
            st.do(pool.tensor_copy(thr[:], ii[:, 0:1]))
            st.do(pool.iota(gi[:], pattern=[[NG // 2, 2]], base=0, channel_multiplier=1))
            st.do(pool.tensor_copy(gf[:], gi[:]))
            assert st.n == 15

        @block.tensor
        def _(pe):
            pe.wait_ge(s_pool, 15)
            for i, (n, k) in enumerate(jobs):
                pe.wait_ge(s_v, n + 1)
                if i >= 2:
                    pe.wait_ge(s_ev, i - 1)
                pe.transpose(ps_t[i % 2][:, 0, :], rowsf[n][:, k, :], c["ident"][:]).then_inc(s_tr, 1)
            pe.wait_ge(s_v, 4)
            pe.matmul(ps_m[0:T, 0:2 * NG], c["ones"][0:1, 0:T], endsf[0:1, :, :].rearrange("a r g -> a (r g)"),
                      start=True, stop=True).then_inc(s_pe, 1)
            pe.wait_ge(s_v, 13)
            pe.matmul(ps_m[0:1, 0:T], cnt[:, 0:1], c["ident"][0:T, 0:T], start=True, stop=True).then_inc(s_pe, 1)
            pe.matmul(ps_m[0:1, T:2 * T + 1], cnt[:, 1:2], tri[:], start=True, stop=True).then_inc(s_pe, 1)
            pe.matmul(ps_m[0:1, 2 * T + 1:3 * T + 1], cnt[:, 1:2], c["ident"][0:T, 0:T], start=True,
                      stop=True).then_inc(s_pe, 1)
            pe.wait_ge(s_v, 14)
            pe.matmul(ps_m[0:NG // 2, 0:3 * T + 1], c["ones"][0:1, 0:NG // 2], rowm[:], start=True,
                      stop=True).then_inc(s_pe, 1)
            pe.wait_ge(s_v, 23)
            for j in range(2):
                pe.matmul(ps_m[0:1, j * (NG // 2):(j + 1) * (NG // 2)], lastc[:, j:j + 1],
                          c["ident"][0:NG // 2, 0:NG // 2], start=True, stop=True).then_inc(s_pe, 1)

        @block.vector
        def _(v):
            v.memset(rows[0][:, RT - 1, :], 0).then_inc(s_fill, 1)
            v.memset(rows[1][:, RT - 1, :], SENT).then_inc(s_fill, 1)
            v.memset(rows[2][:, RT - 1, :], SENT).then_inc(s_fill, 1)
            v.memset(ends[:], SENT).then_inc(s_fill, 1)
            st = Steps(v, s_v)
            v.wait_ge(s_rows, 16 * NDMA)
            for n in range(3):
                st.after(v.tensor_copy(rowsf[n][:], rows[n][:]))
            v.wait_ge(s_ends, 32)
            st.after(v.tensor_copy(endsf[:], ends[:]))
            for i, (n, k) in enumerate(jobs):
                v.wait_ge(s_tr, i + 1)
                to = (c["src"], c["dst"], nxt)[n]
                v.tensor_copy(to[:, k * P:(k + 1) * P], ps_t[i % 2][:, 0, :]).then_inc(s_ev, 1)
            v.wait_ge(s_ev, len(jobs))
            st.after(v.tensor_tensor(c["last"][:], c["dst"][:], nxt[:], ALU.not_equal))
            v.wait_ge(s_pool, 15)
            v.wait_ge(s_pe, 1)
            st.do(v.tensor_scalar(thr_hi[:], thr[:], float(NT), None, ALU.add))
            st.after(v.tensor_scalar(below[:, 0, :], ps_m[0:T, NG:2 * NG], thr[0:T, :], None, ALU.is_lt))
            st.do(v.tensor_scalar(below[:, 1, :], ps_m[0:T, 0:NG], thr_hi[0:T, :], None, ALU.is_lt))
            st.do(v.tensor_reduce(cnt[:], below[:], AX, ALU.add))
            st.do(v.tensor_tensor(cnt[:, 1:2], cnt[:, 1:2], cnt[:, 0:1], ALU.subtract))
            st.do(v.tensor_scalar(cnti[:, 1:2], cnt[:, 1:2], 1.0, 1.0, ALU.max, ALU.add))
            st.do(v.tensor_scalar(cnti[:, 0:1], cnti[:, 1:2], 1, None, ALU.arith_shift_right))
            st.do(v.tensor_copy(cnt[:, 1:2], cnti[:, 0:1]))
            v.wait_ge(s_pe, 4)
            st.do(v.tensor_copy(rowm[:], ps_m[0:1, 0:3 * T + 1]))
            v.wait_ge(s_pe, 5)
            st.do(v.tensor_copy(mb[:], ps_m[0:NG // 2, 0:3 * T + 1]))
            for j in range(2):
                st.after(v.tensor_scalar(mask[:, j, :], mb[:, 0:T], gf[:, j:j + 1], None, ALU.is_le))
                st.after(v.tensor_scalar(seen[:, j, :], mb[:, 0:T], -1.0, gf[:, j:j + 1], ALU.mult, ALU.add))
            st.wait()
            st.do(v.tensor_scalar(seeni[:], seen[:], 2.0, 0.0, ALU.add, ALU.max))
            st.do(v.tensor_scalar(seeni[:], seeni[:], 1, None, ALU.arith_shift_right))
            assert st.n == 21, st.n
            st.do(v.tensor_copy(seen[:], seeni[:]))
            for_j = lambda x: x.rearrange("g (a t) -> g a t", a=1).to_broadcast([NG // 2, 2, T])
            v.tensor_tensor(seen[:], seen[:], for_j(mb[:, 2 * T + 1:3 * T + 1]), ALU.min).then_inc(s_fill, 1)
            v.wait_ge(s_fill, 5)
            v.tensor_tensor(seen[:], seen[:], for_j(mb[:, T:2 * T]), ALU.add).then_inc(s_fill, 1)
            v.wait_ge(s_fill, 6)
            v.tensor_tensor(seen[:], seen[:], mask[:], ALU.mult).then_inc(s_fill, 1)
            v.wait_ge(s_fill, 7)
            st.do(v.tensor_reduce(lastc[:], seen[:], AX, ALU.max))
            st.after(v.tensor_copy(c["meta"][0:1, 0:2 * T + 1], rowm[0:1, 0:2 * T + 1]))
            v.wait_ge(s_pe, 7)
            st.after(v.tensor_copy(c["meta"][0:1, 2 * T + 1:2 * T + 1 + NG], ps_m[0:1, 0:NG]))


def strided(v, first, n):
    w = GC * P
    return v[first:first + (n - 1) * w + 1:w].rearrange("(a n) -> a n", a=1)


def tiles_of(v):
    return v.rearrange("(t p) d -> p t d", p=NT)


def gnn(nc, a, c, dram, sem):
    with ExitStack() as ctx:
        def sb(name, shape, dt=F32):
            return ctx.enter_context(nc.sbuf_tensor(name, shape, dt))

        x0, node_a = c["x0"], c["node_a"]
        W = sb("gnn_w", [P, KD, D + AW])
        Wr = sb("gnn_w_res", [P, KD, D])
        att = sb("att_rows", [P, 2, D])
        prod = sb("att_prod", [P, KD, 2, D])
        gb = sb("ln1_columns", [P, 2, KD])
        bias = sb("gnn_bias", [1, D])
        st6 = sb("stats", [NT, T // 10, 6])
        mvl = sb("mean_var_of_load", [NT, T // 10, 2])
        mv = sb("mean_var", [NT, T, 2])
        rstd = sb("rstd", [NT, T])
        mv2 = sb("mean_var2", [NT, T, 2])
        rstd2 = sb("rstd2", [NT, T])
        n2 = [sb(f"n2_{u}", [NT, D]) for u in range(2)]
        xt = [sb(f"xt_{u}", [P, KD, NT]) for u in range(2)]
        hs = [sb(f"hs_{u}", [NT, D + AW]) for u in range(2)]
        rs = [sb(f"rs_{u}", [NT, D]) for u in range(2)]
        ps_t = [ctx.enter_context(nc.psum_tensor(f"gnn_turned_{u}", [P, KD, P], F32)) for u in range(2)]
        ps_h = [ctx.enter_context(nc.psum_tensor(f"gnn_h_{u}", [P, 512], F32)) for u in range(2)]
        ps_r = [ctx.enter_context(nc.psum_tensor(f"gnn_r_{u}", [P, 512], F32)) for u in range(2)]
        LOADS = 10
        TL = T // LOADS
        s_w, s_att = sem("gnn_weights_in"), sem("att_in")
        s_x = [sem(f"x_in{u}") for u in range(2)]
        s_v, s_fold = sem("gnn_vector"), sem("gnn_folded")
        s_var, s_std = sem("gnn_variances"), sem("gnn_deviations")
        s_n2, s_tr, s_xt = sem("n2_ready"), sem("n2_turned"), sem("xt_ready")
        s_h, s_r, s_hs, s_rs = sem("h_summed"), sem("r_summed"), sem("hs_ready"), sem("rs_ready")
        s_na = sem("node_a_kept")
        s_pass = sem("gnn_passed")
        s_out = [sem(f"gnn_stored{u}") for u in range(2)]
        s_free = sem("gnn_stores_done")
        block = ctx.enter_context(nc.Block())
        xv, hv, av, rv = (tiles_of(t) for t in (a["x"], dram["h"], dram["asrc"], dram["res"]))

        @block.sync
        def _(sp):
            sp.dma_start(att[:, 0, :], spread(a["att_src"].rearrange("h d -> (h d)"))).then_inc(s_att, 16)
            sp.dma_start(att[:, 1, :], spread(a["att_dst"].rearrange("h d -> (h d)"))).then_inc(s_att, 16)
            sp.dma_start(W[:, :, 0:D], a["W"].rearrange("(k p) n -> p k n", p=P)).then_inc(s_att, 16)
            for u in range(2):
                sp.sem_inc(s_x[u], 16)
            with sp.Fori(0, LOADS // 2) as i:
                for u in range(2):
                    sp.wait_ge(s_x[u], 16 * i + 16)
                    part = bass.ds((2 * i + u) * TL, TL)
                    sp.dma_start(x0[:, part, :], xv[:, part, :]).then_inc(s_x[u], 16)
            sp.dma_start(Wr[:], a["W_res"].rearrange("(k p) n -> p k n", p=P)).then_inc(s_w, 16)
            with nc.allow_non_contiguous_dma(reason="columns of the norm's weights"):
                sp.dma_start(gb[:, 0, :], columns(a["ln1_g"], KD)).then_inc(s_w, 16)
                sp.dma_start(gb[:, 1, :], columns(a["ln1_b"], KD)).then_inc(s_w, 16)
            sp.dma_start(bias[:], row(a["bias"])).then_inc(s_w, 16)
            sp.sem_inc(s_free, 2)
            with sp.Fori(0, T // 2) as i:
                for u in range(2):
                    sp.wait_ge(s_hs, 2 * i + u + 1)
                    sp.dma_start(hv[:, 2 * i + u, :], hs[u][:, 0:D]).then_inc(s_out[u], 16)
                    sp.dma_start(av[:, 2 * i + u, :], hs[u][:, D:D + H]).then_inc(s_out[u], 16)
                    sp.wait_ge(s_rs, 2 * i + u + 1)
                    sp.dma_start(rv[:, 2 * i + u, :], rs[u][:]).then_inc(s_out[u], 16)
                for u in range(2):
                    sp.wait_ge(s_out[u], 48 * i + 48)
                sp.sem_inc(s_free, 2)

        @block.vector
        def _(v):
            v.wait_ge(s_att, 48)
            for k in range(KD):
                for s in range(2):
                    v.tensor_tensor(prod[:, k, s, :], W[:, k, 0:D], att[:, s, :], ALU.mult).then_inc(s_fold, 1)
            v.wait_ge(s_fold, 4)
            for k in range(KD):
                v.tensor_reduce(W[:, k, D:D + AW], prod[:, k, :, :].rearrange("p s (h d) -> p (s h) d", d=HD), AX,
                                ALU.add).then_inc(s_fold, 1)
            SB = 2 * TL + 1

            def moments(st, to, n):
                passed(v, s_pass)
                for j in range(TL):
                    st.after(v.bn_stats(st6[:, j, :], x0[:, n * TL + j, :]))
                st.wait()
                passed(v, s_pass)
                for j in range(TL):
                    st.after(v.bn_aggr(mvl[:, j, :], st6[:, j, :]))
                st.wait()
                st.do(v.tensor_copy(to[:, bass.ds(n * TL, TL), :], mvl[:]))

            with v.Fori(0, LOADS // 2) as i:
                for u in range(2):
                    st = Steps(v, s_v, (2 * i + u) * SB)
                    v.wait_ge(s_x[u], 16 * i + 32)
                    moments(st, mv, 2 * i + u)
                    assert st.n == SB
            st = Steps(v, s_v, LOADS * SB)
            v.tensor_scalar(rstd[:], mv[:, :, 1], EPS, None, ALU.add).then_inc(s_var, 1)
            v.wait_ge(s_std, 1)
            st.do(v.reciprocal(rstd[:], rstd[:]))
            with v.Fori(0, LOADS) as n:
                st = Steps(v, s_v, LOADS * SB + 1 + n * (SB + TL))
                for j in range(TL):
                    t = n * TL + j
                    st.after(v.tensor_scalar(x0[:, t, :], x0[:, t, :], mv[:, t, 0:1], rstd[:, bass.ds(t, 1)],
                                             ALU.subtract, ALU.mult))
                st.wait()
                moments(st, mv2, n)
            st = Steps(v, s_v, 2 * LOADS * SB + T + 1)
            v.tensor_scalar(rstd2[:], mv2[:, :, 1], EPS, None, ALU.add).then_inc(s_var, 1)
            v.wait_ge(s_std, 2)
            st.do(v.reciprocal(rstd2[:], rstd2[:]))
            v.sem_inc(s_na, 2)
            with v.Fori(0, T // 2) as i:
                for u in range(2):
                    t = 2 * i + u
                    v.wait_ge(s_tr, t + 1)
                    v.tensor_scalar(n2[u][:], x0[:, t, :], mv2[:, t, 0:1], rstd2[:, bass.ds(t, 1)], ALU.subtract,
                                    ALU.mult).then_inc(s_n2, 1)
                for u in range(2):
                    t = 2 * i + u
                    v.wait_ge(s_r, t + 3)
                    v.wait_ge(s_free, t + 1)
                    v.tensor_copy(rs[u][:], ps_r[u][0:NT, 0:D]).then_inc(s_rs, 1)
                    v.wait_ge(s_hs, t + 1)
                    v.tensor_copy(node_a[:, t, :], hs[u][:, D:D + AW]).then_inc(s_na, 1)

        @block.scalar
        def _(s):
            for n, r in enumerate((rstd, rstd2)):
                s.wait_ge(s_var, n + 1)
                s.activation(r[:], r[:], ACT.Sqrt).then_inc(s_std, 1)
            with s.Fori(0, T // 2) as i:
                for u in range(2):
                    t = 2 * i + u
                    s.wait_ge(s_tr, t + 3)
                    s.wait_ge(s_r, t + 1)
                    for k in range(KD):
                        ins = s.activation(xt[u][:, k, :], ps_t[u][:, k, 0:NT], ACT.Identity, scale=gb[:, 0, k:k + 1],
                                           bias=gb[:, 1, k:k + 1])
                    ins.then_inc(s_xt, 1)
                for u in range(2):
                    t = 2 * i + u
                    s.wait_ge(s_h, t + 1)
                    s.wait_ge(s_free, t + 1)
                    s.wait_ge(s_na, t + 1)
                    s.activation(hs[u][:], ps_h[u][0:NT, 0:D + AW], ACT.Copy).then_inc(s_hs, 1)

        @block.tensor
        def _(pe):
            pe.wait_ge(s_fold, 6)
            pe.wait_ge(s_w, 64)
            pe.sem_inc(s_tr, 2)
            pe.sem_inc(s_r, 2)
            with pe.Fori(0, T // 2) as i:
                for u in range(2):
                    t = 2 * i + u
                    pe.wait_ge(s_n2, t + 1)
                    for k in range(KD):
                        ins = pe.transpose(ps_t[u][:, k, 0:NT], n2[u][:, k * P:(k + 1) * P], c["ident"][0:NT, 0:NT])
                    ins.then_inc(s_tr, 1)
                for u in range(2):
                    t = 2 * i + u
                    pe.wait_ge(s_xt, t + 1)
                    for k in range(KD):
                        ins = pe.matmul(ps_h[u][0:NT, 0:D + AW], xt[u][:, k, :], W[:, k, :], start=(k == 0),
                                        stop=(k == KD - 1))
                    ins.then_inc(s_h, 1)
                    for k in range(KD):
                        pe.matmul(ps_r[u][0:NT, 0:D], xt[u][:, k, :], Wr[:, k, :], start=(k == 0), stop=False)
                    pe.matmul(ps_r[u][0:NT, 0:D], c["ones"][0:1, 0:NT], bias[:], start=False,
                              stop=True).then_inc(s_r, 1)


def tile_steps(eng, meta):
    with eng.Fori(0, T) as t:
        g0 = eng.value_load(meta[0:1, bass.ds(t, 1)], min_val=0, max_val=NG - 1)
        first = eng.value_load(meta[0:1, bass.ds(t + T, 1)], min_val=0, max_val=2 * NG)
        end = eng.value_load(meta[0:1, bass.ds(t + T + 1, 1)], min_val=1, max_val=2 * NG)
        yield t, g0, first, end


def group_of(nc, g0, first, step):
    return nc.s_assert_within(g0 + (step - first) * 2, 0, NG - 1, skip_runtime_bounds_check_because=
                              "a tile's steps end with the group of its last edge or the one after it")


def one_hot(v, out, iota_t, dst, group):
    return v.tensor_tensor(
        out[:],
        iota_t[:].rearrange("p (a n) -> p a n", a=1).to_broadcast([P, GC, NT]),
        dst[:, bass.ds(group * GC, GC)].rearrange("p (c a) -> p c a", a=1).to_broadcast([P, GC, NT]),
        ALU.is_equal)


def mix(nc, a, c, dram, sem):
    with ExitStack() as ctx:
        def sb(name, shape, dt=F32):
            return ctx.enter_context(nc.sbuf_tensor(name, shape, dt))

        def bank(name):
            return ctx.enter_context(nc.psum_tensor(name, [P, 512], F32))

        x0, edge = c["x0"], c["edge"]
        wq = sb("mix_w", [P, KD, 4 * D])
        wo = sb("mix_w_out", [P, KD, D])
        wvt = sb("mix_wv_turned", [P, KD, D])
        bq = sb("mix_bias", [1, 4 * D])
        bcol = sb("mix_bv_column", [P, KD])
        brow = sb("mix_bias_rows", [1, 3, D])
        mean = sb("mix_w_means", [P, KD, 2])
        bmean = sb("mix_b_means", [1, 2])
        zero = sb("mix_zero", [1, 512])
        xs = [sb(f"mix_x{u}", [NT, D]) for u in range(2)]
        xr = [sb(f"mix_x_in{u}", [NT, D]) for u in range(2)]
        xt = [sb(f"mix_xt{u}", [P, KD * NT]) for u in range(2)]
        q2 = sb("mix_q2", [NT, D])
        k2 = sb("mix_k2", [NT, D])
        q4 = sb("mix_q4", [NT, D])
        vs = sb("mix_v", [NT, D])
        k4 = sb("mix_k4", [NT, D])
        sums = sb("mix_sums", [NT, 3])
        root = sb("mix_root", [NT, 1])
        rec = sb("mix_rec", [NT, 2])
        fac = sb("mix_fac", [NT, 1])
        vox = [sb(f"mix_vox{u}", [NT, D]) for u in range(2)]
        qt = [sb(f"mix_qt{u}", [P, KD * NT]) for u in range(2)]
        kn = sb("mix_kn", [P, KD])
        kvn = sb("mix_kvn", [P, KD, D])
        kvt = sb("mix_kvt", [P, KD, D])
        idx = [sb(f"gather_idx{u}", [P, 8], I32) for u in range(2)]
        got = [sb(f"gathered_a{u}", [P, 8, H]) for u in range(2)]
        iota_t = sb("mix_iota_t", [P, NT])
        oh = [sb(f"mix_one_hot{u}", [P, GC, NT]) for u in range(2)]
        oht = [sb(f"mix_one_hot_turned{u}", [NT, GC * P]) for u in range(2)]
        ps_x = [bank(f"mix_ps_x{u}") for u in range(2)]
        ps_qk, ps_v, ps_kv, ps_kn = bank("mix_ps_qk"), bank("mix_ps_v"), bank("mix_ps_kv"), bank("mix_ps_kn")
        ps_q = [bank(f"mix_ps_q{u}") for u in range(2)]
        ps_o = [ps_qk, ps_v]

        s_w, s_prep, s_wpe, s_wev = sem("mix_w_in"), sem("mix_w_vector"), sem("mix_w_tensor"), sem("mix_w_kept")
        s_xr = [sem(f"mix_x_landed{u}") for u in range(2)]
        s_xs, s_xtp, s_xt = sem("mix_xs"), sem("mix_x_turned"), sem("mix_xt")
        s_qk, s_vv = sem("mix_qk_summed"), sem("mix_v_summed")
        s_sq, s_vs, s_root = sem("mix_squared"), sem("mix_v_kept"), sem("mix_rooted")
        s_v = sem("mix_vector")
        s_vox, s_k, s_q2n = sem("mix_vox_ready"), sem("mix_k_ready"), sem("mix_q2n_ready")
        s_kv, s_qtp, s_qt = sem("mix_kv_added"), sem("mix_q_turned"), sem("mix_qt_ready")
        s_st = [sem(f"mix_stored{u}") for u in range(2)]
        s_free = sem("mix_stores_done")
        s_end, s_endv, s_enda = sem("kvo_tensor"), sem("kvo_vector"), sem("kvo_scalar")
        s_idx, s_got = sem("gather_idx_ready"), [sem(f"gathered{u}") for u in range(2)]
        s_keep = sem("gathered_kept")
        s_pass, s_pass_pool = sem("mix_passed"), sem("mix_passed_pool")
        s_it, s_oh, s_turn = sem("mix_iota_t_ready"), sem("mix_one_hot_ready"), sem("mix_one_hot_turned")
        s_oht, s_t1, s_add = sem("mix_one_hot_kept"), sem("targets_summed"), sem("targets_added")
        block = ctx.enter_context(nc.Block())
        xv, vv = tiles_of(a["x"]), tiles_of(dram["vox"])
        qv = dram["q2t"].rearrange("(k p) n -> p k n", p=P)
        WK = 4 + 4 + 3

        @block.sync
        def _(sp):
            sp.dma_start(wq[:, :, 0:3 * D], a["W_qkv"].rearrange("(k p) n -> p k n", p=P)).then_inc(s_w, 16)
            sp.dma_start(wo[:], a["W_out"].rearrange("(k p) n -> p k n", p=P)).then_inc(s_w, 16)
            sp.dma_start(bq[:, 0:3 * D], row(a["b_qkv"])).then_inc(s_w, 16)
            with nc.allow_non_contiguous_dma(reason="the value bias as columns"):
                sp.dma_start(bcol[:], columns(a["b_qkv"][2 * D:3 * D], KD)).then_inc(s_w, 16)
            for n, b in enumerate(("b_out", "ln2_b", "ffn_b2")):
                sp.dma_start(brow[:, n, :], row(a[b])).then_inc(s_w, 16)
            sp.sem_inc(s_free, 2)
            with sp.Fori(0, T // 2) as i:
                for u in range(2):
                    t = 2 * i + u
                    sp.wait_ge(s_vox, t + 1)
                    sp.dma_start(xr[u][:], xv[:, t, :]).then_inc(s_xr[u], 16)
                for u in range(2):
                    t = 2 * i + u
                    sp.wait_ge(s_vox, t + 3)
                    sp.dma_start(vv[:, t, :], vox[u][:]).then_inc(s_st[u], 16)
                    sp.wait_ge(s_qt, t + 1)
                    sp.dma_start(qv[:, :, bass.ds(t * NT, NT)], qt[u][:].rearrange("p (k n) -> p k n", k=KD)
                                 ).then_inc(s_st[u], 16)
                for u in range(2):
                    sp.wait_ge(s_st[u], 32 * i + 32)
                sp.sem_inc(s_free, 2)

        @block.gpsimd
        def _(pool):
            def issue(u, chunk):
                pool.tensor_copy(idx[u][:], c["src"][:, bass.ds(chunk, 8)]).then_inc(s_idx, 1)

            def gathers(u):
                passed(pool, s_pass_pool)
                for j in range(8):
                    pool.indirect_dma_start(got[u][:, j, :], None, dram["asrc"],
                                            bass.IndirectOffsetOnAxis(ap=idx[u][:, j:j + 1], axis=0)
                                            ).then_inc(s_got[u], 16)

            def store(u, chunk):
                pool.tensor_copy(c["a_edge"][:, bass.ds(chunk, 8), :], got[u][:]).then_inc(s_keep, 1)

            pool.tensor_copy(idx[0][:], c["src"][:, 0:8]).then_inc(s_idx, 1)
            pool.wait_ge(s_idx, 1)
            gathers(0)
            with pool.Fori(0, GC * NG // 16) as i:
                issue(1, 16 * i + 8)
                pool.wait_ge(s_idx, 2 * i + 2)
                gathers(1)
                pool.wait_ge(s_got[0], 128 * i + 128)
                store(0, 16 * i)
                issue(0, 16 * i + 16)
                pool.wait_ge(s_idx, 2 * i + 3)
                pool.wait_ge(s_keep, 2 * i + 1)
                gathers(0)
                pool.wait_ge(s_got[1], 128 * i + 128)
                store(1, 16 * i + 8)
                pool.wait_ge(s_keep, 2 * i + 2)
            pool.wait_ge(s_got[0], 128 * (GC * NG // 16) + 128)

        @block.vector
        def _(v):
            v.memset(edge[:], 0.0).then_inc(s_prep, 1)
            v.memset(zero[:], 0.0).then_inc(s_prep, 1)
            v.wait_ge(s_w, 112)
            st = Steps(v, s_prep, 2)
            st.after(v.tensor_reduce(mean[:], wq[:, :, 0:2 * D].rearrange("p k (s n) -> p k s n", s=2), AX, ALU.add))
            st.do(v.tensor_reduce(bmean[:], bq[:, 0:2 * D].rearrange("p (s n) -> p s n", s=2), AX, ALU.add))
            st.after(v.tensor_scalar(mean[:], mean[:], 1.0 / D, None, ALU.mult))
            st.do(v.tensor_scalar(bmean[:], bmean[:], 1.0 / D, None, ALU.mult))
            for s in range(2):
                for k in range(KD):
                    st.after(v.tensor_scalar(wq[:, k, s * D:(s + 1) * D], wq[:, k, s * D:(s + 1) * D],
                                             mean[:, k, s:s + 1], None, ALU.subtract))
                st.after(v.tensor_scalar(bq[:, s * D:(s + 1) * D], bq[:, s * D:(s + 1) * D], bmean[:, s:s + 1], None,
                                         ALU.subtract))
            v.wait_ge(s_wpe, 1)
            v.tensor_copy(wvt[:], ps_qk[:]).then_inc(s_wev, 1)
            v.wait_ge(s_wpe, 2)
            v.tensor_copy(wq[:, :, 3 * D:4 * D], ps_v[:].rearrange("p (k n) -> p k n", k=KD)).then_inc(s_wev, 1)
            v.wait_ge(s_wpe, 3)
            v.tensor_copy(bq[:, 3 * D:4 * D], ps_kn[0:1, 0:D]).then_inc(s_wev, 1)
            v.sem_inc(s_vox, 2)
            SV = 6
            with v.Fori(0, T // 2) as i:
                for u in range(2):
                    t = 2 * i + u
                    v.wait_ge(s_xtp, t + 1)
                    v.tensor_copy(xs[u][:], x0[:, t, :]).then_inc(s_xs, 1)
                for u in range(2):
                    t = 2 * i + u
                    st = Steps(v, s_v, t * SV)
                    v.wait_ge(s_sq, 3 * t + 3)
                    st.do(v.tensor_scalar(rec[:], sums[:, 0:2], EPS_DIV, None, ALU.add))
                    st.do(v.reciprocal(rec[:], rec[:]))
                    v.tensor_scalar(k2[:], k2[:], rec[:, 1:2], None, ALU.mult).then_inc(s_k, 1)
                    v.wait_ge(s_root, t + 1)
                    st.do(v.tensor_scalar(fac[:], root[:], rec[:, 0:1], EPS_NORM, ALU.mult, ALU.max))
                    st.do(v.reciprocal(fac[:], fac[:]))
                    st.do(v.tensor_scalar(fac[:], fac[:], rec[:, 0:1], None, ALU.mult))
                    st.after(v.tensor_scalar(q2[:], q2[:], fac[:, 0:1], None, ALU.mult))
                    st.wait()
                    v.wait_ge(s_k, 2 * t + 1)
                    v.tensor_tensor(k4[:], k2[:], k2[:], ALU.mult).then_inc(s_k, 1)
                    v.wait_ge(s_xr[u], 16 * i + 16)
                    v.wait_ge(s_vs, t + 1)
                    v.wait_ge(s_free, t + 1)
                    v.tensor_tensor(vox[u][:], ps_v[0:NT, D:2 * D], xr[u][:], ALU.add).then_inc(s_vox, 1)
                    assert st.n == SV
            v.wait_ge(s_kv, T + 1)
            v.tensor_copy(kn[:], ps_kn[:, 0:KD]).then_inc(s_endv, 1)
            v.wait_ge(s_enda, 1)
            st = Steps(v, s_endv, 1)
            st.do(v.tensor_scalar(kn[:], kn[:], EPS_NORM, None, ALU.max))
            st.do(v.reciprocal(kn[:], kn[:]))
            for k in range(KD):
                st.after(v.tensor_scalar(kvn[:, k, :], ps_kv[:, k * D:(k + 1) * D], kn[:, k:k + 1], float(N) ** -0.5,
                                         ALU.mult, ALU.mult))
            v.wait_ge(s_end, 1)
            st.after(v.tensor_copy(kvt[:], ps_qk[:]))
            v.wait_ge(s_end, 2)
            st.after(v.tensor_copy(c["kvo"][:], ps_v[:]))
            v.sem_inc(s_turn, 2)
            v.sem_inc(s_add, 2)
            for t, g0, first, end in tile_steps(v, c["meta"]):
                v.tensor_scalar(iota_t[:], c["iota"][:], c["tile_base"][:, bass.ds(t, 1)], None, ALU.add
                                ).then_inc(s_it, 1)
                v.wait_ge(s_it, t + 1)
                passed(v, s_pass)
                with v.Fori(first, end) as s:
                    group = group_of(nc, g0, first, s)
                    for u in range(2):
                        v.wait_ge(s_turn, 2 * s + u + 1)
                        one_hot(v, oh[u], iota_t, c["dst"], group + u).then_inc(s_oh, 1)
                    for u in range(2):
                        v.wait_ge(s_t1, 2 * s + u + 3)
                        v.wait_ge(s_add, 2 * s + u + 2)
                        part = edge[:, bass.ds((group + u) * GC, GC), 0:AW]
                        v.tensor_tensor(part, part, ps_q[u][:, 0:GC * AW].rearrange("p (c n) -> p c n", c=GC), ALU.add
                                        ).then_inc(s_add, 1)

        @block.scalar
        def _(s):
            with s.Fori(0, T // 2) as i:
                for u in range(2):
                    t = 2 * i + u
                    s.wait_ge(s_xtp, t + 3)
                    s.wait_ge(s_vv, t + 1)
                    s.activation(xt[u][:].rearrange("p (k n) -> p k n", k=KD),
                                 ps_x[u][:, 0:KD * P].rearrange("p (k n) -> p k n", k=KD)[:, :, 0:NT], ACT.Copy
                                 ).then_inc(s_xt, 1)
                for u in range(2):
                    t = 2 * i + u
                    s.wait_ge(s_qk, t + 1)
                    s.wait_ge(s_qtp, t + 1)
                    s.wait_ge(s_kv, t + 1)
                    s.activation(q2[:], ps_qk[0:NT, 0:D], ACT.Square, accum_out=sums[:, 0:1]).then_inc(s_sq, 1)
                    s.activation(k2[:], ps_qk[0:NT, D:2 * D], ACT.Square, accum_out=sums[:, 1:2]).then_inc(s_sq, 1)
                    s.wait_ge(s_sq, 3 * t + 1)
                    s.activation(q4[:], q2[:], ACT.Square, accum_out=sums[:, 2:3]).then_inc(s_sq, 1)
                    s.wait_ge(s_sq, 3 * t + 3)
                    s.activation(root[:], sums[:, 2:3], ACT.Sqrt).then_inc(s_root, 1)
                    s.wait_ge(s_vv, t + 3)
                    s.activation(vs[:], ps_v[0:NT, 0:D], ACT.Copy).then_inc(s_vs, 1)
                    s.wait_ge(s_qtp, t + 2)
                    s.wait_ge(s_free, t + 1)
                    s.activation(qt[u][:].rearrange("p (k n) -> p k n", k=KD),
                                 ps_q[u][:, 0:KD * P].rearrange("p (k n) -> p k n", k=KD)[:, :, 0:NT], ACT.Copy
                                 ).then_inc(s_qt, 1)
            s.wait_ge(s_endv, 1)
            s.activation(kn[:], kn[:], ACT.Sqrt).then_inc(s_enda, 1)
            s.sem_inc(s_oht, 2)
            for t, g0, first, end in tile_steps(s, c["meta"]):
                with s.Fori(first, end) as n:
                    for u in range(2):
                        s.wait_ge(s_turn, 2 * n + u + 3)
                        s.wait_ge(s_t1, 2 * n + u + 1)
                        s.activation(oht[u][:], ps_o[u][0:NT, :], ACT.Copy).then_inc(s_oht, 1)

        @block.tensor
        def _(pe):
            pe.wait_ge(s_w, 112)
            for j in range(KD):
                for k in range(KD):
                    ins = pe.transpose(ps_qk[:, j * D + k * P:j * D + (k + 1) * P],
                                       wq[:, k, 2 * D + j * P:2 * D + (j + 1) * P], c["ident"][:])
            ins.then_inc(s_wpe, 1)
            pe.wait_ge(s_wev, 1)
            for k in range(KD):
                for j in range(KD):
                    ins = pe.matmul(ps_v[:, k * D:(k + 1) * D], wvt[:, j, k * P:(k + 1) * P], wo[:, j, :],
                                    start=(j == 0), stop=(j == KD - 1))
            ins.then_inc(s_wpe, 1)
            for j in range(KD):
                pe.matmul(ps_kn[0:1, 0:D], bcol[:, j:j + 1], wo[:, j, :], start=(j == 0), stop=False)
            for n in range(3):
                ins = pe.matmul(ps_kn[0:1, 0:D], c["ones"][0:1, 0:1], brow[:, n, :], start=False, stop=(n == 2))
            ins.then_inc(s_wpe, 1)
            pe.wait_ge(s_wev, 3)
            pe.wait_ge(s_prep, 12)
            pe.matmul(ps_kv[:], c["ones"][0:1, :], zero[:], start=True, stop=True)
            pe.matmul(ps_kn[:, 0:KD], c["ones"][0:1, :], zero[:, 0:KD], start=True, stop=True).then_inc(s_kv, 1)
            pe.sem_inc(s_xtp, 2)
            pe.sem_inc(s_vv, 2)
            pe.sem_inc(s_qtp, 1)
            with pe.Fori(0, T // 2) as i:
                for u in range(2):
                    t = 2 * i + u
                    pe.wait_ge(s_xs, t + 1)
                    for k in range(KD):
                        ins = pe.transpose(ps_x[u][:, k * P:k * P + NT], xs[u][:, k * P:(k + 1) * P],
                                           c["ident"][0:NT, 0:NT])
                    ins.then_inc(s_xtp, 1)
                for u in range(2):
                    t = 2 * i + u
                    pe.wait_ge(s_xt, t + 1)
                    pe.wait_ge(s_vox, t + 2)
                    for ps, at, done in ((ps_qk, 0, s_qk), (ps_v, 2 * D, s_vv)):
                        for k in range(KD):
                            pe.matmul(ps[0:NT, :], xt[u][:, k * NT:(k + 1) * NT], wq[:, k, at:at + 2 * D],
                                      start=(k == 0), stop=False)
                        pe.matmul(ps[0:NT, :], c["ones"][0:1, 0:NT], bq[:, at:at + 2 * D], start=False,
                                  stop=True).then_inc(done, 1)
                    pe.wait_ge(s_k, 2 * t + 2)
                    pe.wait_ge(s_vs, t + 1)
                    for k in range(KD):
                        pe.matmul(ps_kv[:, k * D:(k + 1) * D], k2[:, k * P:(k + 1) * P], vs[:], start=False,
                                  stop=True, skip_group_check=True)
                        ins = pe.matmul(ps_kn[:, k:k + 1], k4[:, k * P:(k + 1) * P], c["ones"][0:NT, 0:1],
                                        start=False, stop=True, skip_group_check=True)
                    ins.then_inc(s_kv, 1)
                    pe.wait_ge(s_v, 6 * t + 6)
                    for k in range(KD):
                        ins = pe.transpose(ps_q[u][:, k * P:k * P + NT], q2[:, k * P:(k + 1) * P],
                                           c["ident"][0:NT, 0:NT])
                    ins.then_inc(s_qtp, 1)
            pe.wait_ge(s_endv, 5)
            for j in range(KD):
                for k in range(KD):
                    ins = pe.transpose(ps_qk[:, j * D + k * P:j * D + (k + 1) * P], kvn[:, k, j * P:(j + 1) * P],
                                       c["ident"][:])
            ins.then_inc(s_end, 1)
            pe.wait_ge(s_endv, 6)
            for k in range(KD):
                for j in range(KD):
                    ins = pe.matmul(ps_v[:, k * D:(k + 1) * D], kvt[:, j, k * P:(k + 1) * P], wo[:, j, :],
                                    start=(j == 0), stop=(j == KD - 1))
            ins.then_inc(s_end, 1)
            pe.sem_inc(s_t1, 2)
            pe.wait_ge(s_endv, 7)
            pe.wait_ge(s_qt, T)
            for t, g0, first, end in tile_steps(pe, c["meta"]):
                with pe.Fori(first, end) as s:
                    for u in range(2):
                        pe.wait_ge(s_oh, 2 * s + u + 1)
                        pe.wait_ge(s_oht, 2 * s + u + 1)
                        for j in range(GC):
                            ins = pe.transpose(ps_o[u][0:NT, j * P:(j + 1) * P], oh[u][:, j, :], c["ident"][:])
                        ins.then_inc(s_turn, 1)
                    for u in range(2):
                        pe.wait_ge(s_oht, 2 * s + u + 3)
                        pe.wait_ge(s_add, 2 * s + u + 1)
                        for j in range(GC):
                            ins = pe.matmul(ps_q[u][:, j * AW:(j + 1) * AW], oht[u][:, j * P:(j + 1) * P],
                                            c["node_a"][:, t, :], start=True, stop=True)
                        ins.then_inc(s_t1, 1)



def soft(nc, a, c, dram, sem):
    with ExitStack() as ctx:
        def sb(name, shape, dt=F32):
            return ctx.enter_context(nc.sbuf_tensor(name, shape, dt))

        LANES = B * H
        edge, a_edge = c["edge"], c["a_edge"]
        xl = sb("scan_x", [LANES, L])
        fwd = sb("scan_fwd", [LANES, L])
        bwd_i = sb("scan_targets", [LANES, L + 2], I32)
        bwd = bwd_i[:, 0:L].bitcast(F32)
        gate = sb("scan_gate", [LANES, L + 1], BF16)
        stage = [sb(f"scan_stage{u}", [P, 2 * LANES]) for u in range(2)]
        cols = sb("scan_cols", [LANES, 4])
        rows = sb("scan_rows", [1, 4, LANES])
        chain = sb("scan_chain", [1, 2, LANES])
        start = sb("scan_start_rows", [1, 2, LANES])
        init = sb("scan_init", [LANES, 2])
        ps = [ctx.enter_context(nc.psum_tensor(f"scan_ps{u}", [P, 512], F32)) for u in range(2)]
        ps_r = ctx.enter_context(nc.psum_tensor("scan_ps_rows", [P, 512], F32))
        s_fill, s_in = sem("scan_filled"), sem("scan_targets_in")
        s_st, s_tr, s_ev = sem("scan_staged"), sem("scan_turned"), sem("scan_kept")
        s_v, s_pe = sem("scan_vector"), sem("scan_tensor")
        s_bs, s_bt, s_be = sem("max_staged"), sem("max_turned"), sem("max_kept")
        s_d, s_e, s_p = sem("scores_ready"), sem("scores_exp"), sem("scores_vector")
        block = ctx.enter_context(nc.Block())
        by_block = lambda t: t[:, 0:B * J, :].rearrange("p (b j) h -> p j b h", b=B)
        mx = xl[:, 0:L].rearrange("p (c h) -> p c h", h=H)
        REST = E - (B - 1) * L
        PIECES = 4
        CQ = B * J // PIECES

        @block.sync
        def _(sp):
            sp.wait_ge(s_fill, 2)
            for b in range(B):
                lo = b * L - 1 if b else 0
                n = L + 2 if 0 < b < B - 1 else (L + 1 if b == 0 else REST + 1)
                at = 1 if b == 0 else 0
                sp.dma_start(bwd_i[b * H:(b + 1) * H, at:at + n], spread(a["dst"][lo:lo + n], H)).then_inc(s_in, 16)
            sp.wait_ge(s_in, 16 * B)

        @block.tensor
        def _(pe):
            pe.sem_inc(s_tr, 2)
            with pe.Fori(0, J // 4) as i:
                for u in range(2):
                    n = 2 * i + u
                    pe.wait_ge(s_st, n + 1)
                    pe.wait_ge(s_ev, n + 1)
                    for j in range(2):
                        ins = pe.transpose(ps[u][:, j * P:(j + 1) * P], stage[u][:, j * LANES:(j + 1) * LANES],
                                           c["ident"][:])
                    ins.then_inc(s_tr, 1)
            pe.wait_ge(s_v, 6)
            for n in range(4):
                ins = pe.matmul(ps_r[0:1, n * LANES:(n + 1) * LANES], cols[:, n:n + 1], c["ident"][:], start=True,
                                stop=True)
            ins.then_inc(s_pe, 1)
            pe.wait_ge(s_v, 7 + 2 * H + 3)
            for n in range(2):
                ins = pe.matmul(ps_r[:, n:n + 1], start[0:1, n, :], c["ones"][0:1, 0:1], start=True, stop=True)
            ins.then_inc(s_pe, 1)
            pe.sem_inc(s_bt, 2)
            with pe.Fori(0, J // 4) as i:
                for u in range(2):
                    n = 2 * i + u
                    pe.wait_ge(s_bs, n + 1)
                    pe.wait_ge(s_be, n + 1)
                    for j in range(2):
                        ins = pe.transpose(ps[u][:, j * LANES:(j + 1) * LANES], stage[u][:, j * P:(j + 1) * P],
                                           c["ident"][:])
                    ins.then_inc(s_bt, 1)

        @block.scalar
        def _(s):
            s.sem_inc(s_ev, 2)
            with s.Fori(0, J // 4) as i:
                for u in range(2):
                    n = 2 * i + u
                    s.wait_ge(s_tr, n + 3)
                    s.activation(xl[:, bass.ds(n * 2 * P, 2 * P)], ps[u][:, 0:2 * P], ACT.Copy).then_inc(s_ev, 1)
            s.sem_inc(s_be, 2)
            s.wait_ge(s_v, 10 + 2 * H + 3)
            with s.Fori(0, J // 4) as i:
                for u in range(2):
                    n = 2 * i + u
                    s.wait_ge(s_bt, n + 3)
                    s.activation(by_block(mx)[:, bass.ds(2 * n, 2), :, :],
                                 ps[u][:, 0:2 * LANES].rearrange("p (j b h) -> p j b h", j=2, b=B), ACT.Copy
                                 ).then_inc(s_be, 1)
            for q in range(PIECES):
                cs = slice(q * CQ, (q + 1) * CQ)
                s.wait_ge(s_d, q + 1)
                s.activation(edge[:, cs, 0:H], a_edge[:, cs, :], ACT.Exp).then_inc(s_e, 1)

        @block.vector
        def _(v):
            v.memset(bwd_i[:, REST + 1:L + 2], SENT).then_inc(s_fill, 1)
            v.memset(bwd_i[:, 0:1], -1).then_inc(s_fill, 1)
            with v.Fori(0, J // 4) as i:
                for u in range(2):
                    n = 2 * i + u
                    v.wait_ge(s_tr, n + 1)
                    v.tensor_copy(stage[u][:].rearrange("p (j b h) -> p j b h", j=2, b=B),
                                  by_block(a_edge)[:, bass.ds(2 * n, 2), :, :]).then_inc(s_st, 1)
            st = Steps(v, s_v)
            v.wait_ge(s_in, 16 * B)
            st.do(v.tensor_tensor(gate[:], bwd_i[:, 1:L + 2], bwd_i[:, 0:L + 1], ALU.not_equal))
            st.do(v.tensor_scalar(gate[:], gate[:], -BIG, None, ALU.mult))
            v.wait_ge(s_ev, J // 2 + 2)

            def scans(first):
                st.after(v.tensor_tensor_scan(fwd[:], gate[:, 0:L], xl[:], first[0], ALU.add, ALU.max))
                st.after(v.tensor_tensor_scan(bwd[:, ::-1], gate[:, 1:L + 1][:, ::-1], xl[:, ::-1], first[1],
                                              ALU.add, ALU.max))

            scans((-BIG, -BIG))
            st.wait()
            v.tensor_copy(cols[:, 0:1], fwd[:, L - 1:L]).then_inc(s_p, 1)
            v.tensor_copy(cols[:, 2:3], bwd[:, 0:1]).then_inc(s_p, 1)
            st.after(v.tensor_reduce(cols[:, 1:2], gate[:, 0:L], AX, ALU.min))
            v.wait_ge(s_p, 2)
            st.after(v.tensor_reduce(cols[:, 3:4], gate[:, 1:L + 1], AX, ALU.min))
            v.wait_ge(s_pe, 1)
            st.do(v.tensor_copy(rows[:], ps_r[0:1, 0:4 * LANES]))
            for n in range(2):
                for h in range(H):
                    lane = lambda r: r[:, h:LANES:H] if n == 0 else r[:, h:LANES:H][:, ::-1]
                    st.after(v.tensor_tensor_scan(lane(chain[:, n, :]), lane(rows[:, 2 * n + 1, :]),
                                                  lane(rows[:, 2 * n, :]), -BIG, ALU.add, ALU.max))
            st.do(v.memset(start[:], -BIG))
            st.after(v.tensor_copy(start[:, 0, H:LANES], chain[:, 0, 0:LANES - H]))
            st.after(v.tensor_copy(start[:, 1, 0:LANES - H], chain[:, 1, H:LANES]))
            v.wait_ge(s_pe, 2)
            v.tensor_copy(init[:], ps_r[:, 0:2]).then_inc(s_p, 1)
            v.wait_ge(s_p, 3)
            scans((init[:, 0:1], init[:, 1:2]))
            st.wait()
            st.do(v.tensor_tensor(fwd[:], fwd[:], bwd, ALU.max))
            with v.Fori(0, J // 4) as i:
                for u in range(2):
                    n = 2 * i + u
                    v.wait_ge(s_bt, n + 1)
                    v.tensor_copy(stage[u][:], fwd[:, bass.ds(n * 2 * P, 2 * P)]).then_inc(s_bs, 1)
            v.wait_ge(s_be, J // 2 + 2)
            st = Steps(v, s_p, 3)
            for q in range(PIECES):
                cs = slice(q * CQ, (q + 1) * CQ)
                m, z, asn, ad = mx[:, cs, :], a_edge[:, cs, :], edge[:, cs, 0:H], edge[:, cs, H:AW]
                st.after(v.tensor_tensor(z, z, ad, ALU.add))
                st.do(v.tensor_tensor(m, m, asn, ALU.max))
                st.do(v.tensor_tensor(m, m, ad, ALU.add))
                st.after(v.scalar_tensor_tensor(z, z, SLOPE, z, ALU.mult, ALU.max))
                st.do(v.scalar_tensor_tensor(m, m, SLOPE, m, ALU.mult, ALU.max))
                v.tensor_tensor(z, z, m, ALU.subtract).then_inc(s_d, 1)
                last = c["last"][:, cs].rearrange("p (c a) -> p c a", a=1)
                st.after(v.tensor_tensor(ad, m, last.to_broadcast([P, CQ, H]), ALU.mult))
                st.after(v.tensor_copy(edge[:, cs, AW:EW], last))


def main(nc, a, c, dram, sem):
    with ExitStack() as ctx:
        def sb(name, shape, dt=F32):
            return ctx.enter_context(nc.sbuf_tensor(name, shape, dt))

        edge, ones, ident = c["edge"], c["ones"], c["ident"]
        PR = 2 * NT
        w1f = sb("ffn_w1", [P, KD, FF])
        w2f = sb("ffn_w2", [P, FFC, D])
        w1 = sb("moe_w1", [P, X, KD, XH])
        w2 = sb("moe_w2", [P, X, XC, D])
        wr = sb("moe_wr", [P, KD, X])
        b1f = sb("ffn_b1", [P, FFC])
        b1 = sb("moe_b1", [P, X, XC])
        b2 = sb("moe_b2", [X, D])
        br = sb("moe_br", [1, X])
        g2row = sb("ln2_g_rows", [NT, D])
        gb = sb("norm_columns", [P, 4, KD])
        zero = sb("main_zero", [1, SW])
        ring = sb("ring", [P, RING * GC, D])
        idx = sb("ring_idx", [P, RING, GC], I32)
        iota_t = [sb(f"main_iota_t{u}", [P, NT]) for u in range(2)]
        oh = [sb(f"main_one_hot{u}", [P, GC, NT]) for u in range(2)]
        msg = [sb(f"weighted{u}", [P, GC, D]) for u in range(2)]
        hs = sb("own_h", [NT, 2, D])
        acc = sb("own_res", [NT, 2, D])
        vox = sb("own_vox", [NT, 2, D])
        q2t = sb("own_q2", [P, KD, PR])
        nb = sb("normed", [NT, 2, D])
        x1 = sb("x1", [NT, 2, D])
        xt = sb("turned", [P, KD, PR])
        hid = sb("hidden", [P, 2 * XC, PR])
        s8 = sb("self_score", [NT, 2, H])
        l8 = sb("self_max", [NT, 2, H])
        e8 = sb("self_exp", [NT, 2, H])
        d8 = sb("self_den", [NT, 2, H])
        none = sb("no_edge", [NT, 2, 1])
        st6 = sb("main_stats", [NT, 2, 6])
        mv = sb("main_mean_var", [NT, 2, 2])
        rstd = sb("main_rstd", [NT, 2])
        lg = sb("logits", [NT, 2, X])
        top = sb("top8", [NT, 2, 8])
        topi = sb("top8_idx", [NT, 2, 8], U32)
        topf = sb("top8_lane", [NT, 2, 8])
        tw = sb("top_weights", [NT, 2, 2])
        wf = sb("expert_weights", [NT, 2, X])
        wf2 = sb("expert_weights2", [NT, 2, X])
        wt = sb("expert_weights_turned", [X, PR])
        ag = ctx.enter_context(nc.psum_tensor("sums", [P, 2, 512], F32))
        ph = [ctx.enter_context(nc.psum_tensor(f"hidden_ps{u}", [P, 512], F32)) for u in range(2)]
        py = [ctx.enter_context(nc.psum_tensor(f"out_ps{u}", [P, 2, D], F32)) for u in range(2)]
        pm = ctx.enter_context(nc.psum_tensor("turned_ps", [P, 2, KD, P], F32))
        pl = ctx.enter_context(nc.psum_tensor("logits_ps", [P, 512], F32))

        s_w1, s_w2 = sem("main_small_in"), sem("main_experts_in")
        s_zero = sem("main_zeroed")
        s_idx, s_land, s_landed = sem("ring_idx_ready"), [sem(f"ring_land{r}") for r in range(RING)], sem("ring_landed")
        s_it, s_msg, s_used = sem("main_iota_t_ready"), sem("weighted_ready"), sem("weighted_used")
        s_agr = sem("sums_read")
        s_ld, s_lv = sem("own_rows_in"), sem("own_vox_in")
        s_hfree, s_vfree = sem("own_rows_free"), sem("own_vox_free")
        s_v = sem("main_vector")
        s_es, s_esd, s_var, s_std = sem("self_ready"), sem("self_exp_done"), sem("main_var"), sem("main_std")
        s_n, s_tr, s_xt = sem("normed_ready"), sem("normed_turned"), sem("turned_kept")
        s_ps, s_hid = sem("hidden_summed"), sem("hidden_ready")
        s_y, s_yd = sem("out_summed"), sem("out_added")
        s_lg, s_dif, s_dex, s_wf, s_wtp, s_wt = (sem("logits_summed"), sem("top_gap"), sem("top_gap_exp"),
                                                sem("weights_ready"), sem("weights_turned"), sem("weights_kept"))
        s_out = sem("rows_stored")
        s_pass, s_pass_pool = sem("main_passed"), sem("main_passed_pool")
        block = ctx.enter_context(nc.Block())
        G = T // 2
        NY = X + 2
        NH = FFC + X * XC
        both = lambda v: v.rearrange("(g u p) d -> p (g u) d", u=2, p=NT)

        @block.sync
        def _(sp):
            with nc.allow_non_contiguous_dma(reason="columns of biases and norms"):
                for n, v in enumerate(("ln2_g", "ln2_b", "moe_gamma", "moe_beta")):
                    sp.dma_start(gb[:, n, :], columns(a[v], KD)).then_inc(s_w1, 16)
                sp.dma_start(b1f[:], columns(a["ffn_b1"], FFC)).then_inc(s_w1, 16)
                sp.dma_start(b1[:].rearrange("p e c -> p (e c)"), a["moe_b1"].rearrange("e (c p) -> p (e c)", p=P)
                             ).then_inc(s_w1, 16)
            sp.dma_start(wr[:], a["moe_Wr"].rearrange("(k p) n -> p k n", p=P)).then_inc(s_w1, 16)
            sp.dma_start(b2[:], a["moe_b2"]).then_inc(s_w1, 16)
            sp.dma_start(br[:], row(a["moe_br"])).then_inc(s_w1, 16)
            sp.dma_start(g2row[:], spread(a["ln2_g"], NT)).then_inc(s_w1, 16)
            sp.dma_start(w1f[:], a["ffn_w1"].rearrange("(k p) n -> p k n", p=P)).then_inc(s_w1, 16)
            sp.dma_start(w2f[:], a["ffn_w2"].rearrange("(k p) n -> p k n", p=P)).then_inc(s_w1, 16)
            for e in range(X):
                sp.dma_start(w1[:, e, :, :], a["moe_W1"][e].rearrange("(k p) n -> p k n", p=P)).then_inc(s_w2, 16)
                sp.dma_start(w2[:, e, :, :], a["moe_W2"][e].rearrange("(k p) n -> p k n", p=P)).then_inc(s_w2, 16)
            with sp.Fori(0, G) as g:
                sp.wait_ge(s_hfree, g + 1)
                sp.dma_start(hs[:], both(dram["h"])[:, bass.ds(2 * g, 2), :]).then_inc(s_ld, 16)
                sp.dma_start(acc[:], both(dram["res"])[:, bass.ds(2 * g, 2), :]).then_inc(s_ld, 16)
                sp.wait_ge(s_vfree, g + 1)
                sp.dma_start(vox[:], both(dram["vox"])[:, bass.ds(2 * g, 2), :]).then_inc(s_lv, 16)
                sp.dma_start(q2t[:], dram["q2t"].rearrange("(k p) n -> p k n", p=P)[:, :, bass.ds(g * PR, PR)]
                             ).then_inc(s_lv, 16)

        @block.gpsimd
        def _(pool):
            def fill(r, group, free):
                pool.tensor_copy(idx[:, r, :], c["src"][:, bass.ds(group * GC, GC)]).then_inc(s_idx, 1)
                if free is not None:
                    pool.wait_ge(s_msg, free)
                pool.wait_ge(s_idx, group + 1)
                passed(pool, s_pass_pool)
                for j in range(GC):
                    pool.indirect_dma_start(ring[:, r * GC + j, :], None, dram["h"],
                                            bass.IndirectOffsetOnAxis(ap=idx[:, r, j:j + 1], axis=0)
                                            ).then_inc(s_land[r], 16)

            def landed(r, uses):
                pool.wait_ge(s_land[r], 16 * GC * uses)
                pool.sem_inc(s_landed, 1)

            for r in range(RING):
                fill(r, r, None)
                if r:
                    landed(r - 1, 1)
            LOOPS = -(-(NG + 1) // RING)
            with pool.Fori(1, LOOPS) as i:
                for r in range(RING):
                    group = i * RING + r
                    at = c["meta"][0:1, bass.ds(group + (2 * T + 1 - RING), 1)]
                    steps = pool.value_load(at, min_val=1, max_val=2 * NG)
                    fill(r, group, steps * 2)
                    landed(r - 1 if r else RING - 1, i + 1 if r else i)
            landed(RING - 1, LOOPS)

        @block.vector
        def _(v):
            v.memset(zero[:], 0.0).then_inc(s_zero, 1)
            v.sem_inc(s_agr, 1)
            v.sem_inc(s_hfree, 1)
            v.sem_inc(s_vfree, 1)
            v.sem_inc(s_yd, 2)
            v.sem_inc(s_out, 16)
            SV = 52
            with v.Fori(0, G) as g:
                for u in range(2):
                    t = 2 * g + u
                    g0 = v.value_load(c["meta"][0:1, bass.ds(t, 1)], min_val=0, max_val=NG - 1)
                    first = v.value_load(c["meta"][0:1, bass.ds(t + T, 1)], min_val=0, max_val=2 * NG)
                    end = v.value_load(c["meta"][0:1, bass.ds(t + T + 1, 1)], min_val=1, max_val=2 * NG)
                    v.tensor_scalar(iota_t[u][:], c["iota"][:], c["tile_base"][:, bass.ds(t, 1)], None, ALU.add
                                    ).then_inc(s_it, 1)
                    v.wait_ge(s_it, t + 1)
                    passed(v, s_pass)
                    with v.Fori(first, end) as s:
                        group = group_of(nc, g0, first, s)
                        for k in range(2):
                            v.wait_ge(s_used, 2 * s + k + 1)
                            one_hot(v, oh[k], iota_t[u], c["dst"], group + k)
                            v.wait_ge(s_landed, (group + k + 1) & 1023)
                            slot = (group + k) % RING
                            v.tensor_tensor(
                                msg[k][:].rearrange("p c (h d) -> p c h d", h=H),
                                ring[:, bass.ds(slot * GC, GC), :].rearrange("p c (h d) -> p c h d", h=H),
                                edge[:, bass.ds((group + k) * GC, GC), 0:H].rearrange("p c (h a) -> p c h a", a=1
                                                                                       ).to_broadcast([P, GC, H, HD]),
                                ALU.mult).then_inc(s_msg, 1)
                    last_end = end
                st = Steps(v, s_v, g * SV)
                agn = ag[0:NT, :, :]
                na = c["node_a"][:, bass.ds(2 * g, 2), :]
                st.do(v.tensor_tensor(s8[:], na[:, :, 0:H], na[:, :, H:AW], ALU.add))
                st.do(v.scalar_tensor_tensor(s8[:], s8[:], SLOPE, s8[:], ALU.mult, ALU.max))
                v.wait_ge(s_used, last_end * 2 + 2)
                st.do(v.tensor_scalar(none[:], agn[:, :, SW - 1:SW], -1.0, 1.0, ALU.mult, ALU.add))
                st.do(v.tensor_tensor(l8[:], s8[:], none[:].to_broadcast([NT, 2, H]), ALU.mult))
                st.do(v.tensor_tensor(l8[:], l8[:], agn[:, :, D + H:D + AW], ALU.add))
                v.tensor_tensor(s8[:], s8[:], l8[:], ALU.subtract).then_inc(s_es, 1)
                v.wait_ge(s_ld, 32 * g + 32)
                v.wait_ge(s_esd, g + 1)
                st.after(v.tensor_tensor(d8[:], agn[:, :, D:D + H], e8[:], ALU.add))
                heads = lambda x: x.rearrange("p u (h d) -> p u h d", h=H)
                wide = lambda x: x[:].rearrange("p u (h a) -> p u h a", a=1).to_broadcast([NT, 2, H, HD])
                st.do(v.tensor_tensor(heads(hs[:]), heads(hs[:]), wide(e8), ALU.mult))
                st.after(v.reciprocal(d8[:], d8[:]))
                v.tensor_tensor(hs[:], agn[:, :, 0:D], hs[:], ALU.add).then_inc(s_agr, 1)
                st.wait()
                v.wait_ge(s_agr, g + 2)
                st.do(v.tensor_tensor(heads(hs[:]), heads(hs[:]), wide(d8), ALU.mult))
                st.do(v.tensor_tensor(acc[:], acc[:], hs[:], ALU.add))

                def norm(x, to, nth, ready):
                    for u in range(2):
                        st.after(v.bn_stats(st6[:, u, :], x[:, u, :]))
                    st.wait()
                    passed(v, s_pass)
                    for u in range(2):
                        st.after(v.bn_aggr(mv[:, u, :], st6[:, u, :]))
                    st.wait()
                    v.tensor_scalar(rstd[:], mv[:, :, 1], EPS, None, ALU.add).then_inc(s_var, 1)
                    v.wait_ge(s_std, 3 * g + nth)
                    st.do(v.reciprocal(rstd[:], rstd[:]))
                    for u in range(2):
                        ins = v.tensor_scalar(to[:, u, :], x[:, u, :], mv[:, u, 0:1], rstd[:, u:u + 1], ALU.subtract,
                                              ALU.mult)
                        if u and ready is not None:
                            ins.then_inc(ready, 1)
                        else:
                            st.after(ins)
                    if ready is None:
                        st.wait()

                norm(acc, nb, 1, s_n)
                v.wait_ge(s_n, 2 * g + 1)
                v.sem_inc(s_hfree, 1)
                st.wait()
                v.wait_ge(s_lv, 32 * g + 32)
                v.wait_ge(s_out, 16 * g + 16)
                st.do(v.tensor_tensor(x1[:], nb[:],
                                      g2row[:].rearrange("p (a d) -> p a d", a=1).to_broadcast([NT, 2, D]), ALU.mult))
                st.do(v.tensor_tensor(x1[:], x1[:], vox[:], ALU.add))
                v.wait_ge(s_y, NY * g + 2)
                v.sem_inc(s_vfree, 1)
                v.tensor_tensor(x1[:], x1[:], py[0][0:NT, :, :], ALU.add).then_inc(s_yd, 1)
                v.wait_ge(s_yd, NY * g + 3)
                norm(x1, nb, 2, None)
                norm(nb, nb, 3, s_n)
                v.wait_ge(s_lg, g + 1)
                st.do(v.tensor_copy(lg[:], pl[0:NT, 0:2 * X].rearrange("p (u e) -> p u e", u=2)))
                passed(v, s_pass)
                for u in range(2):
                    st.after(v.max(top[:, u, :], lg[:, u, :]))
                st.wait()
                v.tensor_tensor(tw[:, :, 1:2], top[:, :, 1:2], top[:, :, 0:1], ALU.subtract).then_inc(s_dif, 1)
                for u in range(2):
                    st.after(v.max_index(topi[:, u, :], top[:, u, :], lg[:, u, :]))
                st.wait()
                st.after(v.tensor_copy(topf[:], topi[:]))
                v.wait_ge(s_dex, g + 1)
                st.do(v.tensor_scalar(tw[:, :, 0:1], tw[:, :, 1:2], 1.0, None, ALU.add))
                st.do(v.reciprocal(tw[:, :, 0:1], tw[:, :, 0:1]))
                st.do(v.tensor_tensor(tw[:, :, 1:2], tw[:, :, 1:2], tw[:, :, 0:1], ALU.mult))
                for u in range(2):
                    st.after(v.tensor_scalar(wf[:, u, :], c["lane8"][0:NT, :], topf[:, u, 0:1], tw[:, u, 0:1],
                                             ALU.is_equal, ALU.mult))
                    st.after(v.tensor_scalar(wf2[:, u, :], c["lane8"][0:NT, :], topf[:, u, 1:2], tw[:, u, 1:2],
                                             ALU.is_equal, ALU.mult))
                st.wait()
                v.tensor_tensor(wf[:], wf[:], wf2[:], ALU.add).then_inc(s_wf, 1)
                v.wait_ge(s_wtp, g + 1)
                v.tensor_copy(wt[:], pl[0:X, 2 * X:2 * X + PR]).then_inc(s_wt, 1)
                v.wait_ge(s_y, NY * g + 3)
                v.tensor_tensor(x1[:], x1[:], py[1][0:NT, :, :], ALU.add).then_inc(s_yd, 1)
                for e in range(X):
                    v.wait_ge(s_y, NY * g + 4 + e)
                    v.wait_ge(s_yd, NY * g + 4 + e)
                    for u in range(2):
                        ins = v.scalar_tensor_tensor(x1[:, u, :], py[e % 2][0:NT, u, :], wf[:, u, e:e + 1],
                                                     x1[:, u, :], ALU.mult, ALU.add)
                        if u == 0:
                            st.after(ins)
                    ins.then_inc(s_yd, 1)
                    st.wait()
                assert st.n == SV, st.n

        @block.scalar
        def _(s):
            s.sem_inc(s_hid, 2)
            s.wait_ge(s_w1, 16 * 12)
            with s.Fori(0, G) as g:
                s.wait_ge(s_es, g + 1)
                s.activation(e8[:], s8[:], ACT.Exp).then_inc(s_esd, 1)

                def sqrt(nth):
                    s.wait_ge(s_var, 3 * g + nth)
                    s.activation(rstd[:], rstd[:], ACT.Sqrt).then_inc(s_std, 1)

                def keep(nth):
                    s.wait_ge(s_tr, 2 * g + nth + 1)
                    for k in range(KD):
                        ins = s.activation(xt[:, k, :].rearrange("p (u n) -> p u n", u=2), pm[:, :, k, 0:NT],
                                           ACT.Identity, scale=gb[:, 2 * nth, k:k + 1],
                                           bias=gb[:, 2 * nth + 1, k:k + 1])
                    ins.then_inc(s_xt, 1)

                def hidden(n, slot, bias, f):
                    s.wait_ge(s_ps, NH * g + n + 1)
                    s.activation(hid[:, slot, :], ph[n % 2][:, 0:PR], f, bias=bias).then_inc(s_hid, 1)

                sqrt(1)
                keep(0)
                s.wait_ge(s_y, NY * g + 1)
                for n in range(FFC):
                    hidden(n, n, b1f[:, n:n + 1], ACT.Gelu_apprx_tanh)
                sqrt(2)
                sqrt(3)
                keep(1)
                for e in range(X):
                    s.wait_ge(s_y, NY * g + (2 if e < 2 else e + 2))
                    for n in range(XC):
                        hidden(FFC + e * XC + n, (e % 2) * XC + n, b1[:, e, n:n + 1], ACT.Gelu)
                    if e == 0:
                        s.wait_ge(s_dif, g + 1)
                        s.activation(tw[:, :, 1:2], tw[:, :, 1:2], ACT.Exp).then_inc(s_dex, 1)
                s.wait_ge(s_yd, NY * g + NY + 2)
                s.dma_start(both(a["out"])[:, bass.ds(2 * g, 2), :], x1[:]).then_inc(s_out, 16)
            s.wait_ge(s_out, 16 * G + 16)

        @block.tensor
        def _(pe):
            pe.wait_ge(s_zero, 1)
            pe.wait_ge(s_w1, 16 * 12)
            pe.sem_inc(s_used, 2)
            pe.sem_inc(s_y, 1)
            with pe.Fori(0, G) as g:
                pe.wait_ge(s_agr, g + 1)
                for u in range(2):
                    t = 2 * g + u
                    first = pe.value_load(c["meta"][0:1, bass.ds(t + T, 1)], min_val=0, max_val=2 * NG)
                    end = pe.value_load(c["meta"][0:1, bass.ds(t + T + 1, 1)], min_val=1, max_val=2 * NG)
                    g0 = pe.value_load(c["meta"][0:1, bass.ds(t, 1)], min_val=0, max_val=NG - 1)
                    pe.matmul(ag[0:NT, u, 0:SW], ones[0:1, 0:NT], zero[:], start=True, stop=True)
                    with pe.Fori(first, end) as s:
                        group = group_of(nc, g0, first, s)
                        for k in range(2):
                            pe.wait_ge(s_msg, 2 * s + k + 1)
                            for j in range(GC):
                                pe.matmul(ag[0:NT, u, 0:D], oh[k][:, j, :], msg[k][:, j, :], start=False, stop=True,
                                          skip_group_check=True)
                                ins = pe.matmul(ag[0:NT, u, D:SW], oh[k][:, j, :],
                                                edge[:, (group + k) * GC + j, :], start=False,
                                                stop=True, skip_group_check=True)
                            ins.then_inc(s_used, 1)

                def turn(nth):
                    pe.wait_ge(s_n, 2 * g + nth + 1)
                    for u in range(2):
                        for k in range(KD):
                            ins = pe.transpose(pm[:, u, k, 0:NT], nb[:, u, k * P:(k + 1) * P], ident[0:NT, 0:NT])
                    ins.then_inc(s_tr, 1)

                def hidden(n, w):
                    pe.wait_ge(s_hid, NH * g + n + 1)
                    for k in range(KD):
                        ins = pe.matmul(ph[n % 2][:, 0:PR], w[k], xt[:, k, :], start=(k == 0), stop=(k == KD - 1))
                    ins.then_inc(s_ps, 1)

                def out(y, n, slots, w, more=()):
                    pe.wait_ge(s_yd, NY * g + y + 1)
                    parts = list(more)
                    for i, slot in enumerate(slots):
                        parts.append((lambda u, slot=slot: hid[:, slot, u * NT:(u + 1) * NT], w[i], n + i))
                    for i, (lhs, rhs, chunk) in enumerate(parts):
                        if chunk is not None:
                            pe.wait_ge(s_hid, NH * g + chunk + 3)
                        for u in range(2):
                            ins = pe.matmul(py[y % 2][0:NT, u, :], lhs(u), rhs, start=(i == 0 and u == 0),
                                            stop=True, skip_group_check=True)
                    ins.then_inc(s_y, 1)

                turn(0)
                pe.wait_ge(s_xt, 2 * g + 1)
                for n in range(FFC):
                    hidden(n, [w1f[:, k, n * P:(n + 1) * P] for k in range(KD)])
                pe.wait_ge(s_lv, 32 * g + 32)
                out(0, 0, range(FFC), [w2f[:, n, :] for n in range(FFC)],
                    [(lambda u, k=k: q2t[:, k, u * NT:(u + 1) * NT], c["kvo"][:, k, :], None) for k in range(KD)])
                turn(1)
                pe.wait_ge(s_xt, 2 * g + 2)
                for u in range(2):
                    for k in range(KD):
                        pe.matmul(pl[0:NT, u * X:(u + 1) * X], xt[:, k, u * NT:(u + 1) * NT], wr[:, k, :],
                                  start=(k == 0), stop=False)
                    ins = pe.matmul(pl[0:NT, u * X:(u + 1) * X], ones[0:1, 0:NT], br[:], start=False, stop=True)
                ins.then_inc(s_lg, 1)

                def expert_hidden(e):
                    for n in range(XC):
                        hidden(FFC + e * XC + n, [w1[:, e, k, n * P:(n + 1) * P] for k in range(KD)])

                pe.wait_ge(s_w2, 16 * 2 * X)
                expert_hidden(0)
                expert_hidden(1)
                pe.wait_ge(s_wf, g + 1)
                for u in range(2):
                    ins = pe.transpose(pl[0:X, 2 * X + u * NT:2 * X + (u + 1) * NT], wf[:, u, :], ident[0:NT, 0:NT])
                ins.then_inc(s_wtp, 1)
                pe.wait_ge(s_wt, g + 1)
                out(1, 0, [], [], [(lambda u: wt[:, u * NT:(u + 1) * NT], b2[:], None)])
                for e in range(X):
                    out(2 + e, FFC + e * XC, [(e % 2) * XC + n for n in range(XC)], [w2[:, e, n, :] for n in range(XC)])
                    if e + 2 < X:
                        expert_hidden(e + 2)


_INS = ['x', 'src', 'dst', 'L0_gnn_W', 'L0_gnn_att_src', 'L0_gnn_att_dst', 'L0_gnn_bias', 'L0_gnn_W_res',
        'L0_gnn_ln1_g', 'L0_gnn_ln1_b', 'L0_gnn_ln2_g', 'L0_gnn_ln2_b', 'L0_gnn_ffn_w1', 'L0_gnn_ffn_b1',
        'L0_gnn_ffn_w2', 'L0_gnn_ffn_b2', 'L0_mix_W_qkv', 'L0_mix_b_qkv', 'L0_mix_W_out', 'L0_mix_b_out',
        'L0_ffn_gamma', 'L0_ffn_beta', 'L0_ffn_Wr', 'L0_ffn_br', 'L0_ffn_W1', 'L0_ffn_b1', 'L0_ffn_W2', 'L0_ffn_b2']


def kernel(**inputs):
    import concourse.bacc as _bacc
    from concourse.bass_utils import run_bass_kernel_spmd as _run

    nc = _bacc.Bacc("TRN2", target_bir_lowering=False, num_devices=1)
    arrays, args = {}, {}
    for name in _INS:
        v = np.ascontiguousarray(inputs[name])
        arrays[f"in_{name}"] = v
        args[short(name)] = nc.dram_tensor(f"in_{name}", v.shape, mybir.dt.from_np(v.dtype), kind="ExternalInput").ap()
    args["out"] = nc.dram_tensor("out_rows", (N, D), F32, kind="ExternalOutput").ap()
    gps_layer(nc, args)
    r = _run(nc, [arrays], core_ids=[0])
    return r.results[0]["out_rows"]
```
